# Optimizing a Trainium2 kernel written in Bass

```python
import numpy as np
import jax
import jax.numpy as jnp

def _softmax(x, axis=-1):
    return jax.nn.softmax(x, axis=axis)

def _gelu(x):
    return jax.nn.gelu(x, approximate=True)

def _silu(x):
    return jax.nn.silu(x)

def _sigmoid(x):
    return jax.nn.sigmoid(x)

def _layernorm(x, axis=-1, eps=1e-05):
    m = jnp.mean(x, axis=axis, keepdims=True)
    v = jnp.var(x, axis=axis, keepdims=True)
    return (x - m) / jnp.sqrt(v + eps)

def _scatter_add(tgt, idx, src, axis=0):
    return tgt.at[idx].add(src)

def _segment_sum(src, seg, n):
    return jax.ops.segment_sum(src, seg, n)
kernel_name = 'mk_adj_preln_d1_adj_r2_cf4238'

def setup_inputs(seed: int=0):
    np.random.seed(seed)
    _w = jnp.asarray

    def _rec_inputs():
        import jax
        import jax.numpy as jnp
        _gk = jax.random.key(seed)
        x = -0.0002037 + 1 * jax.random.normal(jax.random.fold_in(_gk, 1), (5000, 128), jnp.float32)
        _a = jax.random.bernoulli(jax.random.fold_in(_gk, 2), 0.0004, (5000, 5000))
        _a = jnp.logical_or(_a, jnp.swapaxes(_a, -1, -2))
        _a = jnp.logical_or(_a, jnp.eye(5000, dtype=bool))
        _af = _a.astype(jnp.float32)
        adj = _af
        return (x, adj)
    x, adj = _rec_inputs()

    def _L0_gnn_setup():
        import jax, jax.numpy as jnp
        import numpy as np
        N = 5000
        F = 128
        C = 16
        AL = 0.1
        EPS = 1e-12
        key = jax.random.key(seed)
        k1, k2, k3, k4 = jax.random.split(key, 4)
        A = (jax.random.uniform(k1, (N, N)) > 0.99).astype(jnp.float32)
        x = jax.random.normal(k2, (N, F), dtype=jnp.float32)
        h0 = jax.random.normal(k3, (N, F), dtype=jnp.float32)
        labels = jax.random.randint(k4, (N,), 0, C)
        y = jax.nn.one_hot(labels, C, dtype=jnp.float32)
        return {'input': x, 'A': A, 'h0': h0, 'y': y}
    _L0_gnn_all = _L0_gnn_setup()
    _L0_gnn_in = {k: v for k, v in _L0_gnn_all.items() if k in ('h0', 'y')}
    del _L0_gnn_all
    return {'x': x, 'adj': adj, 'L0_gnn_h0': _L0_gnn_in['h0'], 'L0_gnn_y': _L0_gnn_in['y']}

def reference(x, adj, L0_gnn_h0, L0_gnn_y):
    import jax
    import jax.numpy as jnp

    def _L0_gnn_ref(input, A, h0, y):
        import jax, jax.numpy as jnp
        import numpy as np
        N = 5000
        F = 128
        C = 16
        AL = 0.1
        EPS = 1e-12
        adj = A * (y @ y.T)
        row_l1 = jnp.maximum(jnp.sum(jnp.abs(adj), axis=1, keepdims=True), EPS)
        adj = adj / row_l1
        support = adj @ input
        return (1.0 - AL) * support + AL * h0
    h = jnp.maximum(_layernorm(x, axis=-1), 0.0)
    x = x + _L0_gnn_ref(h, adj, L0_gnn_h0, L0_gnn_y)
    return x

_drawn_inputs = setup_inputs


def setup_inputs(seed=0):
    import zlib

    import numpy as np

    out = dict(_drawn_inputs(seed))
    spreads = {}
    factors = {}
    for name, (base, spread) in spreads.items():
        noise = np.random.default_rng([zlib.crc32(name.encode()), seed]).standard_normal(out[name].shape)
        drawn = base * np.exp(spread * noise) if base else spread * noise
        out[name] = jnp.asarray(drawn.astype(out[name].dtype))
    for name, factor in factors.items():
        out[name] = (out[name] * factor).astype(out[name].dtype)
    return out
```

```python
from contextlib import ExitStack

import concourse.bass as bass
from concourse import mybir


def build_masked_adjacency(nc, x, adj_t, h0, y, y_t, out):
    F32, BF16, F16 = mybir.dt.float32, mybir.dt.bfloat16, mybir.dt.float16
    U8, U16, I32 = mybir.dt.uint8, mybir.dt.uint16, mybir.dt.int32
    ALU, ACT, AX = mybir.AluOpType, mybir.ActivationFunctionType, mybir.AxisListType

    N, F = x.shape
    C = y.shape[1]
    P = 128
    NB = N // P
    FULL = NB * P
    REM = N - FULL
    B = NB + 1
    BANKS = 8
    GW = BANKS * P
    NG = B // BANKS
    LW = N - (NG - 1) * GW
    ROUND = [4, 3, 3, 3]
    RB = sum(ROUND)
    START = [sum(ROUND[:q]) for q in range(len(ROUND))]
    Q = len(ROUND)
    ROUNDS = NB // RB
    CHUNKS = Q * ROUNDS
    ON_VECTOR = (5, 11)
    W = 2 * F + 1
    SCALE = 2048.0
    ALPHA, EPS_L1, EPS_LN = 0.1, 1e-12, 1e-5
    PART = 10
    LAB_N = 500
    RK = 500
    RC = REM * N // RK
    BAD = 2 * CHUNKS
    ON_SCALAR = CHUNKS - len(ON_VECTOR)
    BADS = NG * BAD + 5

    with ExitStack() as ctx:
        def sb(name, shape, dt):
            return ctx.enter_context(nc.sbuf_tensor(name, shape, dt))

        def sem(name):
            return ctx.enter_context(nc.semaphore(name))

        a_ring = sb("a_ring", [P, RB, GW], F32)
        m_ring = sb("m_ring", [P, RB, GW], BF16)
        x_sb = sb("x_sb", [P, B, F], F32)
        base = sb("base", [P, B, F], F32)
        h_sb = sb("h_sb", [P, B, W], F16)
        label_row = sb("label_row", [P, N], BF16)
        scratch = sb("scratch", [P, N], F32)
        m_rem = sb("m_rem", [P, N], BF16)
        a_rem_check = sb("a_rem_check", [RC, RK], F32)
        y_sb = sb("y_sb", [P, B, C], F32)
        y_tmp = sb("y_tmp", [P, B, C], F32)
        class_row = sb("class_row", [P, C], F32)
        class_col = sb("class_col", [C, 1], I32)
        class_w = sb("class_w", [C, P], BF16)
        label_col = sb("label_col", [P, B], F32)
        one_hot_sum = sb("one_hot_sum", [P, B], F32)
        stats = sb("stats", [P, B, 6], F32)
        mean = sb("mean", [P, B], F32)
        var = sb("var", [P, B], F32)
        tmp = sb("tmp", [P, B], F32)
        root = sb("root", [P, B], F32)
        rstd = sb("rstd", [P, B], F32)
        shift = sb("shift", [P, B], F32)
        bad = sb("bad", [P, BADS], F32)
        bad_seen = sb("bad_seen", [P, BADS], F32)
        bad_p = sb("bad_p", [P, 1], F32)
        ones = sb("ones", [P, P], F32)
        flag = sb("flag", [P, 1], I32)
        recip = sb("recip", [P, BANKS], F32)
        l1 = sb("l1", [P, BANKS], F32)
        out_sb = sb("out_sb", [P, BANKS, F], F32)
        ps = ctx.enter_context(nc.psum_tensor("ps", [P, BANKS, 512], F32))
        g_adj, g_m, g_abs, g_h, g_rows = (a_ring[:, s, 0:P] for s in range(5))
        g_yi, g_yj = a_ring[0:C, 5, 0:P], a_ring[0:C, 6, 0:P]
        a_rem = scratch[0:REM, :]
        EDGE = [0, max(ROUND) * GW // 2, (max(ROUND) + min(ROUND)) * GW // 2]
        low_junk = scratch[:, EDGE[0]:EDGE[1] // 2].bitcast(U8)
        sign_junk = scratch[:, EDGE[1] // 2:EDGE[1]].bitcast(U8)
        dve_junk = scratch[:, EDGE[1]:EDGE[2]].bitcast(BF16)
        part_sb = scratch[:, EDGE[2]:EDGE[2] + GW].rearrange("p (k f) -> p k f", k=BANKS)
        yt_sb = m_ring[0:C, :, :].rearrange("c s i -> c (s i)")[:, 0:2 * N]

        y_loaded, yt_loaded, x_loaded, h0_loaded = sem("y_loaded"), sem("yt_loaded"), sem("x_loaded"), sem("h0_loaded")
        rem_loaded, rem_check_loaded = sem("rem_loaded"), sem("rem_check_loaded")
        a_loaded = [sem(f"a_loaded{q}") for q in range(Q)]
        tails_cleared, classes_ready, class_w_ready = sem("tails_cleared"), sem("classes_ready"), sem("class_w_ready")
        operands_cleared = sem("operands_cleared")
        labels_spread, label_row_ready = sem("labels_spread"), sem("label_row_ready")
        pool_step, base_ready = sem("pool_step"), sem("base_ready")
        var_ready, root_ready, affine_ready, relu_ready = sem("var_ready"), sem("root_ready"), sem("affine_ready"), sem("relu_ready")
        h_ready, rem_masked, masked = sem("h_ready"), sem("rem_masked"), sem("masked")
        low_checked, vector_checked = sem("low_checked"), sem("vector_checked")
        chunk_checked, m_used = sem("chunk_checked"), sem("m_used")
        bank_summed, bank_read = sem("bank_summed"), sem("bank_read")
        out_free, out_stored, tail_stored = sem("out_free"), sem("out_stored"), sem("tail_stored")
        dve_step, bad_cleared = sem("dve_step"), sem("bad_cleared")
        l1_ready, recip_ready, hi_added = sem("l1_ready"), sem("recip_ready"), sem("hi_added")
        bad_ready, bad_summed, flag_ready = sem("bad_ready"), sem("bad_summed"), sem("flag_ready")
        g_yi_loaded, g_loaded, g_summed = sem("g_yi_loaded"), sem("g_loaded"), sem("g_summed")
        g_yy_ready, g_m_step, g_m_ready = sem("g_yy_ready"), sem("g_m_step"), sem("g_m_ready")
        g_l1_ready, g_recip_ready = sem("g_l1_ready"), sem("g_recip_ready")
        g_rows_ready, g_stored = sem("g_rows_ready"), sem("g_stored")

        block = ctx.enter_context(nc.Block())

        def checks_through(c):
            return sum(k not in ON_VECTOR for k in range(c + 1))

        def value(eng, v):
            return v if isinstance(v, int) else eng.snap(eng.to_reg(v))

        def groups(eng, body):
            with eng.Fori(0, NG - 1) as g:
                body(g, GW)
            body(NG - 1, LW)

        def steps_of_block(eng, b, body):
            body(b * B, NB, REM)
            with eng.Fori(0, NB - 1) as t:
                body(b * B + t + 1, t, P)
            body(b * B + NB, NB - 1, P)

        def blocks(eng, body):
            with eng.Fori(0, NB) as b:
                body(b, P)
            body(NB, REM)

        def if_needed(eng, path):
            eng.wait_ge(flag_ready, 1)
            found = eng.value_load(flag[0:1, 0:1], min_val=0, max_val=1)
            with eng.If(found > 0):
                path()

        @block.sync
        def _(sp):
            sp.dma_start(yt_sb.bitcast(F32), y_t[:, :]).then_inc(yt_loaded, 16)
            sp.dma_start(y_sb[:, 0:NB, :], y[0:FULL, :].rearrange("(b p) c -> p b c", p=P)).then_inc(y_loaded, 16)
            sp.dma_start(x_sb[:, 0:NB, :], x[0:FULL, :].rearrange("(b p) f -> p b f", p=P)).then_inc(x_loaded, 16)
            sp.wait_ge(tails_cleared, 3)
            sp.dma_start(y_sb[0:REM, NB, :], y[FULL:N, :]).then_inc(y_loaded, 16)
            sp.dma_start(x_sb[0:REM, NB, :], x[FULL:N, :]).then_inc(x_loaded, 16)
            sp.dma_start(a_rem, adj_t[FULL:N, :]).then_inc(rem_loaded, 16)
            sp.dma_start(base[:, 0:NB, :], h0[0:FULL, :].rearrange("(b p) f -> p b f", p=P)).then_inc(h0_loaded, 16)
            sp.dma_start(base[0:REM, NB, :], h0[FULL:N, :]).then_inc(h0_loaded, 16)
            sp.dma_start(a_rem_check[:, :], adj_t[FULL:N, :].rearrange("r (s k) -> (r s) k", k=RK)).then_inc(rem_check_loaded, 16)

            def load_group(g, w):
                for r in range(ROUNDS):
                    for q in range(Q):
                        c = r * Q + q
                        before = c - Q if r else c - Q + CHUNKS
                        masked_before = value(sp, (g + 1) * NB + (r - 1) * RB + START[q] + ROUND[q])
                        checked_before = value(sp, (g + (1 if r else 0)) * ON_SCALAR + checks_through(before))
                        sp.wait_ge(masked, masked_before)
                        sp.wait_ge(chunk_checked, checked_before)
                        j = (r * RB + START[q]) * P
                        sp.dma_start(a_ring[:, START[q]:START[q] + ROUND[q], 0:w],
                                     adj_t[j:j + ROUND[q] * P, bass.ds(g * GW, w)].rearrange("(b p) i -> p b i", p=P),
                                     ).then_inc(a_loaded[q], 16)

            groups(sp, load_group)

            def general_path():
                sp.wait_ge(out_stored, 16 * (NG - 1))
                sp.wait_ge(tail_stored, 32)
                sp.sem_inc(g_stored, 16)
                sp.sem_inc(g_summed, 1)

                def load_block(b, w):
                    sp.dma_start(g_yi[:, 0:w], y_t[:, bass.ds(b * P, w)]).then_inc(g_yi_loaded, 16)

                    def load_step(n, t, rows):
                        sp.wait_ge(g_summed, n + 1)
                        sp.dma_start(g_adj[0:rows, 0:w], adj_t[bass.ds(t * P, rows), bass.ds(b * P, w)]).then_inc(g_loaded, 16)
                        sp.dma_start(g_yj[:, 0:rows], y_t[:, bass.ds(t * P, rows)]).then_inc(g_loaded, 16)

                    steps_of_block(sp, b, load_step)
                    sp.wait_ge(g_rows_ready, b + 2)
                    sp.dma_start(out[bass.ds(b * P, w), :], g_rows[0:w, :]).then_inc(g_stored, 16)

                blocks(sp, load_block)
                sp.wait_ge(g_stored, 16 * (B + 1))

            if_needed(sp, general_path)

        @block.gpsimd
        def _(pool):
            nc.gpsimd.memset(x_sb[:, NB, :], 0.0).then_inc(tails_cleared, 1)
            nc.gpsimd.memset(y_sb[:, NB, :], 0.0).then_inc(tails_cleared, 1)
            nc.gpsimd.memset(base[:, NB, :], 0.0).then_inc(tails_cleared, 1)
            nc.gpsimd.iota(class_col[:, :], pattern=[[0, 1]], base=1, channel_multiplier=1).then_inc(pool_step, 1)
            pool.wait_ge(pool_step, 1)
            nc.gpsimd.tensor_copy(class_w[:, :], class_col[:, 0:1].to_broadcast([C, P])).then_inc(class_w_ready, 1)
            for c in range(C):
                last = nc.gpsimd.memset(class_row[:, c:c + 1], c + 1.0)
            last.then_inc(classes_ready, 1)
            nc.gpsimd.memset(m_rem[:, :], 0.0).then_inc(operands_cleared, 1)
            nc.gpsimd.memset(h_sb[:, :, 2 * F:W], 1.0).then_inc(operands_cleared, 1)
            nc.gpsimd.memset(ones[:, :], 1.0).then_inc(operands_cleared, 1)
            pool.wait_ge(h0_loaded, 32)
            nc.gpsimd.tensor_scalar(base[:, :, :], base[:, :, :], ALPHA, 0.0, ALU.mult, ALU.add).then_inc(pool_step, 1)
            pool.wait_ge(pool_step, 2)
            pool.wait_ge(x_loaded, 32)
            nc.gpsimd.tensor_tensor(base[:, :, :], base[:, :, :], x_sb[:, :, :], ALU.add).then_inc(base_ready, 1)

            pool.sem_inc(out_free, 1)
            with pool.Fori(0, NG - 1) as g:
                pool.wait_ge(bank_read, (g + 2) * BANKS)
                pool.dma_start(out[bass.ds(g * GW, GW), :].rearrange("(b p) f -> p b f", p=P),
                               out_sb[:, :, :]).then_inc(out_stored, 16)
                pool.wait_ge(out_stored, 16 * (g + 1))
                pool.sem_inc(out_free, 1)
            pool.wait_ge(bank_read, (NG + 1) * BANKS)
            pool.dma_start(out[(NG - 1) * GW:FULL, :].rearrange("(b p) f -> p b f", p=P),
                           out_sb[:, 0:BANKS - 1, :]).then_inc(tail_stored, 16)
            pool.dma_start(out[FULL:N, :], out_sb[0:REM, BANKS - 1, :]).then_inc(tail_stored, 16)
            pool.wait_ge(out_stored, 16 * (NG - 1))
            pool.wait_ge(tail_stored, 32)

        @block.scalar
        def _(act):
            act.sem_inc(chunk_checked, ON_SCALAR)
            for k in range(N // LAB_N):
                act.wait_ge(labels_spread, k + 1)
                nc.scalar.activation(label_row[:, k * LAB_N:(k + 1) * LAB_N], ps[:, k % BANKS, 0:LAB_N],
                                     ACT.Copy).then_inc(label_row_ready, 1)
            act.wait_ge(var_ready, 1)
            nc.scalar.activation(root[:, :], var[:, :], ACT.Sqrt).then_inc(root_ready, 1)
            act.wait_ge(affine_ready, 1)
            act.wait_ge(base_ready, 1)
            for b in range(B):
                made = nc.scalar.activation(x_sb[:, b, :], x_sb[:, b, :], ACT.Relu, bias=shift[:, b:b + 1],
                                            scale=rstd[:, b:b + 1])
                if b % PART == PART - 1:
                    made.then_inc(relu_ready, 1)

            act.wait_ge(bad_cleared, 1)
            act.wait_ge(rem_check_loaded, 16)
            act.wait_ge(rem_masked, 1)
            rb = NG * BAD
            nc.scalar.activation(low_junk[0:RC, 0:RK], a_rem_check[:, :].bitcast(U16)[:, 0:2 * RK:2], ACT.Copy,
                                 accum_out=bad[0:RC, rb:rb + 1]).then_inc(low_checked, 1)
            nc.scalar.activation(sign_junk[0:RC, 0:RK], a_rem_check[:, :], ACT.Relu, scale=-1.0,
                                 accum_out=bad[0:RC, rb + 1:rb + 2]).then_inc(low_checked, 1)

            def check_group(g, w):
                for r in range(ROUNDS):
                    for q in range(Q):
                        c = r * Q + q
                        if c in ON_VECTOR:
                            continue
                        done = checks_through(c - 1)
                        nb = ROUND[q]
                        blocks = slice(START[q], START[q] + nb)
                        act.wait_ge(a_loaded[q], 16 * (g * ROUNDS + r + 1))
                        act.wait_ge(low_checked, g * ON_SCALAR + done + 2)
                        nc.scalar.activation(low_junk[:, 0:nb * w].rearrange("p (b i) -> p b i", b=nb),
                                             a_ring[:, :, :].bitcast(U16)[:, blocks, 0:2 * w:2], ACT.Copy,
                                             accum_out=bad[:, bass.ds(g * BAD + 2 * c, 1)]).then_inc(low_checked, 1)
                        act.wait_ge(chunk_checked, (g + 1) * ON_SCALAR + done)
                        nc.scalar.activation(sign_junk[:, 0:nb * w].rearrange("p (b i) -> p b i", b=nb),
                                             a_ring[:, blocks, 0:w], ACT.Relu, scale=-1.0,
                                             accum_out=bad[:, bass.ds(g * BAD + 2 * c + 1, 1)]).then_inc(chunk_checked, 1)

            groups(act, check_group)

        @block.tensor
        def _(pe):
            pe.wait_ge(yt_loaded, 16)
            pe.wait_ge(class_w_ready, 1)
            for k in range(N // LAB_N):
                if k >= BANKS:
                    pe.wait_ge(label_row_ready, k - BANKS + 1)
                nc.tensor.matmul(ps[:, k % BANKS, 0:LAB_N], class_w[:, :],
                                 yt_sb[:, 2 * k * LAB_N + 1:2 * (k + 1) * LAB_N:2],
                                 start=True, stop=True).then_inc(labels_spread, 1)
            pe.wait_ge(label_row_ready, N // LAB_N)
            pe.wait_ge(operands_cleared, 3)
            pe.wait_ge(rem_masked, 1)
            pe.wait_ge(h_ready, B // PART)

            def sum_group(g, w):
                sizes = [min(P, w - P * k) for k in range(BANKS)]
                for k, m in enumerate(sizes):
                    pe.wait_ge(bank_read, g * BANKS + k + 1)
                    nc.tensor.matmul(ps[0:m, k, 0:W], m_rem[:, bass.ds(g * GW + k * P, m)], h_sb[:, NB, :],
                                     start=True, stop=False)
                for r in range(ROUNDS):
                    for s in range(RB):
                        b = r * RB + s
                        pe.wait_ge(masked, (g + 1) * NB + b + 1)
                        for k, m in enumerate(sizes):
                            mm = nc.tensor.matmul(ps[0:m, k, 0:W], m_ring[:, s, k * P:k * P + m], h_sb[:, b, :],
                                                  start=False, stop=(b == NB - 1))
                            if b == NB - 1:
                                mm.then_inc(bank_summed, 1)
                        if b < NB - 1:
                            mm.then_inc(m_used, 1)

            groups(pe, sum_group)

            pe.wait_ge(bad_ready, 1)
            pe.wait_ge(bank_read, (NG + 1) * BANKS)
            nc.tensor.matmul(ps[:, 0, 0:1], ones[:, :], bad_p[:, :], start=True, stop=True).then_inc(bad_summed, 1)

            def general_path():
                pe.sem_inc(g_rows_ready, 1)

                def sum_block(b, w):
                    pe.wait_ge(g_yi_loaded, 16 * (b + 1))

                    def sum_step(n, t, rows):
                        first, last = rows == REM, isinstance(t, int) and t == NB - 1
                        pe.wait_ge(g_loaded, 32 * (n + 1))
                        nc.tensor.matmul(ps[:, 0, 0:P], g_yj, g_yi, start=True,
                                         stop=True).then_inc(g_yy_ready, 1)
                        pe.wait_ge(g_m_ready, n + 1)
                        if first:
                            pe.wait_ge(g_rows_ready, b + 1)
                        nc.tensor.matmul(ps[:, 1, 0:F], g_m[0:rows, :], g_h[0:rows, :], start=first, stop=last)
                        nc.tensor.matmul(ps[:, 2, 0:1], g_abs[0:rows, :], ones[0:rows, 0:1], start=first,
                                         stop=last).then_inc(g_summed, 1)

                    steps_of_block(pe, b, sum_step)

                blocks(pe, sum_block)

            if_needed(pe, general_path)

        @block.vector
        def _(dve):
            steps = [0]

            def wait_own(ins):
                steps[0] += 1
                ins.then_inc(dve_step, 1)
                dve.wait_ge(dve_step, steps[0])

            dve.sem_inc(masked, NB)
            dve.sem_inc(bank_read, BANKS)
            nc.vector.memset(bad[:, :], 0.0).then_inc(bad_cleared, 1)
            dve.wait_ge(bad_cleared, 1)

            dve.wait_ge(y_loaded, 32)
            dve.wait_ge(classes_ready, 1)
            wait_own(nc.vector.tensor_tensor(y_tmp[:, :, :], y_sb[:, :, :],
                                             class_row[:, :].rearrange("p (o c) -> p o c", o=1).to_broadcast([P, B, C]), ALU.mult))
            wait_own(nc.vector.reduce_sum(label_col[:, :], y_tmp[:, :, :], AX.X))
            yb = NG * BAD + 2
            nc.vector.scalar_tensor_tensor(y_tmp[:, :, :], y_sb[:, :, :], 1.0, y_sb[:, :, :], ALU.is_equal,
                                           ALU.not_equal, accum_out=bad[:, yb:yb + 1])
            wait_own(nc.vector.reduce_sum(one_hot_sum[:, :], y_sb[:, :, :], AX.X))
            nc.vector.tensor_scalar(tmp[:, 0:NB], one_hot_sum[:, 0:NB], 1.0, 0.0, ALU.not_equal, ALU.add,
                                    accum_out=bad[:, yb + 1:yb + 2])
            wait_own(nc.vector.tensor_scalar(tmp[0:REM, NB:B], one_hot_sum[0:REM, NB:B], 1.0, 0.0, ALU.not_equal, ALU.add,
                                             accum_out=bad[0:REM, yb + 2:yb + 3]))

            dve.wait_ge(x_loaded, 32)
            for b in range(B):
                st = nc.vector.bn_stats(stats[:, b, :], x_sb[:, b, :])
            wait_own(st)
            wait_own(nc.vector.tensor_tensor(mean[:, :], stats[:, :, 1], stats[:, :, 4], ALU.subtract))
            wait_own(nc.vector.tensor_tensor(var[:, :], mean[:, :], mean[:, :], ALU.mult))
            wait_own(nc.vector.scalar_tensor_tensor(var[:, :], var[:, :], F / 4.0, stats[:, :, 2], ALU.mult, ALU.add))
            wait_own(nc.vector.tensor_tensor(var[:, :], var[:, :], stats[:, :, 5], ALU.add))
            nc.vector.tensor_scalar(var[:, :], var[:, :], 1.0 / F, EPS_LN, ALU.mult, ALU.add).then_inc(var_ready, 1)
            wait_own(nc.vector.tensor_tensor(mean[:, :], stats[:, :, 1], stats[:, :, 4], ALU.add))
            dve.wait_ge(root_ready, 1)
            wait_own(nc.vector.reciprocal(rstd[:, :], root[:, :]))
            wait_own(nc.vector.tensor_tensor(tmp[:, :], rstd[:, :], rstd[:, :], ALU.mult))
            wait_own(nc.vector.tensor_tensor(tmp[:, :], tmp[:, :], var[:, :], ALU.mult))
            wait_own(nc.vector.tensor_scalar(tmp[:, :], tmp[:, :], -0.5 * SCALE, 1.5 * SCALE, ALU.mult, ALU.add))
            wait_own(nc.vector.tensor_tensor(rstd[:, :], rstd[:, :], tmp[:, :], ALU.mult))
            nc.vector.scalar_tensor_tensor(shift[:, :], mean[:, :], -0.5, rstd[:, :], ALU.mult,
                                           ALU.mult).then_inc(affine_ready, 1)
            dve.wait_ge(label_row_ready, N // LAB_N)
            dve.wait_ge(operands_cleared, 1)
            dve.wait_ge(rem_loaded, 16)
            nc.vector.scalar_tensor_tensor(m_rem[0:REM, :], label_row[0:REM, :], label_col[0:REM, NB:B], a_rem,
                                           ALU.is_equal, ALU.mult).then_inc(rem_masked, 1)
            for part in range(B // PART):
                bs = slice(part * PART, (part + 1) * PART)
                dve.wait_ge(relu_ready, part + 1)
                wait_own(nc.vector.tensor_copy(h_sb[:, bs, 0:F], x_sb[:, bs, :]))
                nc.vector.tensor_tensor(h_sb[:, bs, F:2 * F], x_sb[:, bs, :], h_sb[:, bs, 0:F],
                                        ALU.subtract).then_inc(h_ready, 1)

            def mask_group(g, w):
                labels = label_row[:, bass.ds(g * GW, w)]
                for r in range(ROUNDS):
                    for q in range(Q):
                        c = r * Q + q
                        dve.wait_ge(a_loaded[q], 16 * (g * ROUNDS + r + 1))
                        if c in ON_VECTOR:
                            dve.wait_ge(vector_checked, g * len(ON_VECTOR) + ON_VECTOR.index(c) + 1)
                            data = a_ring[:, START[q]:START[q] + ROUND[q], 0:w]
                            nc.vector.scalar_tensor_tensor(
                                dve_junk[:, 0:ROUND[q] * w].rearrange("p (b i) -> p b i", b=ROUND[q]),
                                data, 1.0, data, ALU.is_equal, ALU.not_equal,
                                accum_out=bad[:, bass.ds(g * BAD + 2 * c, 1)]).then_inc(vector_checked, 1)
                        for s in range(START[q], START[q] + ROUND[q]):
                            b = r * RB + s
                            if r:
                                dve.wait_ge(m_used, (g + 1) * (NB - 1) + b - RB + 1)
                            elif s < RB - 1:
                                dve.wait_ge(m_used, g * (NB - 1) + NB - RB + s + 1)
                            nc.vector.scalar_tensor_tensor(m_ring[:, s, 0:w], labels, label_col[:, b:b + 1],
                                                           a_ring[:, s, 0:w], ALU.is_equal, ALU.mult).then_inc(masked, 1)
                dve.wait_ge(bank_summed, (g + 1) * BANKS)
                nc.vector.tensor_scalar(l1[:, :], ps[:, :, 2 * F], EPS_L1, SCALE / (1.0 - ALPHA), ALU.max,
                                        ALU.mult).then_inc(l1_ready, 1)
                dve.wait_ge(l1_ready, g + 1)
                nc.vector.reciprocal(recip[:, :], l1[:, :]).then_inc(recip_ready, 1)
                dve.wait_ge(recip_ready, g + 1)
                for k in range(BANKS):
                    nc.vector.scalar_tensor_tensor(part_sb[:, k, :], ps[:, k, 0:F], recip[:, k:k + 1],
                                                   base[:, bass.ds(g * BANKS + k, 1), :].rearrange("p o f -> p (o f)"),
                                                   ALU.mult, ALU.add).then_inc(hi_added, 1)
                dve.wait_ge(out_free, g + 1)
                for k in range(BANKS):
                    dve.wait_ge(hi_added, g * BANKS + k + 1)
                    nc.vector.scalar_tensor_tensor(out_sb[:, k, :], ps[:, k, F:2 * F], recip[:, k:k + 1],
                                                   part_sb[:, k, :], ALU.mult, ALU.add).then_inc(bank_read, 1)

            dve.sem_inc(m_used, NB - 1)
            dve.sem_inc(vector_checked, 1)
            dve.wait_ge(base_ready, 1)
            groups(dve, mask_group)

            dve.wait_ge(chunk_checked, (NG + 1) * ON_SCALAR)
            dve.wait_ge(vector_checked, NG * len(ON_VECTOR) + 1)
            wait_own(nc.vector.tensor_scalar(bad_seen[:, :], bad[:, :], 0.0, None, ALU.not_equal))
            nc.vector.reduce_sum(bad_p[:, :], bad_seen[:, :], AX.X).then_inc(bad_ready, 1)
            dve.wait_ge(bad_summed, 1)
            nc.vector.tensor_scalar(flag[:, :], ps[:, 0, 0:1], 0.0, None, ALU.is_gt).then_inc(flag_ready, 1)

            def general_path():
                def mask_block(b, w):
                    def mask_step(n, t, rows):
                        dve.wait_ge(g_yy_ready, n + 1)
                        nc.vector.tensor_tensor(g_m[0:rows, :], g_adj[0:rows, :], ps[0:rows, 0, 0:P], ALU.mult).then_inc(g_m_step, 1)
                        nc.vector.tensor_tensor(g_h[0:rows, :], h_sb[0:rows, bass.ds(t, 1), 0:F].rearrange("p o f -> p (o f)"),
                                                h_sb[0:rows, bass.ds(t, 1), F:2 * F].rearrange("p o f -> p (o f)"), ALU.add)
                        dve.wait_ge(g_m_step, n + 1)
                        nc.vector.scalar_tensor_tensor(g_abs[0:rows, :], g_m[0:rows, :], -1.0, g_m[0:rows, :], ALU.mult, ALU.max).then_inc(g_m_ready, 1)

                    steps_of_block(dve, b, mask_step)
                    dve.wait_ge(g_summed, (b + 1) * B + 1)
                    nc.vector.tensor_scalar(l1[:, 0:1], ps[:, 2, 0:1], EPS_L1, SCALE / (1.0 - ALPHA), ALU.max,
                                            ALU.mult).then_inc(g_l1_ready, 1)
                    dve.wait_ge(g_l1_ready, b + 1)
                    nc.vector.reciprocal(recip[:, 0:1], l1[:, 0:1]).then_inc(g_recip_ready, 1)
                    dve.wait_ge(g_recip_ready, b + 1)
                    dve.wait_ge(g_stored, 16 * (b + 1))
                    nc.vector.scalar_tensor_tensor(g_rows[:, :], ps[:, 1, 0:F], recip[:, 0:1],
                                                   base[:, bass.ds(b, 1), :].rearrange("p o f -> p (o f)"),
                                                   ALU.mult, ALU.add).then_inc(g_rows_ready, 1)

                blocks(dve, mask_block)

            if_needed(dve, general_path)


_OUT_SHAPE, _OUT_DTYPE = (5000, 128), "float32"


def kernel(x, adj, L0_gnn_h0, L0_gnn_y):
    import numpy as np
    import concourse.bacc as bacc
    from concourse.bass_utils import run_bass_kernel_spmd

    nc = bacc.Bacc("TRN2", target_bir_lowering=False, num_devices=1)
    x, adj, h0, y = (np.asarray(a) for a in (x, adj, L0_gnn_h0, L0_gnn_y))
    arrays = {
        "x": np.ascontiguousarray(x),
        "adj_t": np.ascontiguousarray(adj.T),
        "h0": np.ascontiguousarray(h0),
        "y": np.ascontiguousarray(y),
        "y_t": np.ascontiguousarray(y.T),
    }
    handles = [nc.dram_tensor(name, a.shape, mybir.dt.from_np(a.dtype), kind="ExternalInput").ap()
               for name, a in arrays.items()]
    handles.append(nc.dram_tensor("result", _OUT_SHAPE, mybir.dt.from_np(np.dtype(_OUT_DTYPE)), kind="ExternalOutput").ap())
    build_masked_adjacency(nc, *handles)
    got = run_bass_kernel_spmd(nc, [arrays], core_ids=[0])
    return got.results[0]["result"]
```

```python
from contextlib import ExitStack

import concourse.bass as bass
from concourse import mybir


def build_masked_adjacency(nc, x, adj_t, h0, y, y_t, out, *, N):
    F32, BF16, F16 = mybir.dt.float32, mybir.dt.bfloat16, mybir.dt.float16
    U8, U16, I32 = mybir.dt.uint8, mybir.dt.uint16, mybir.dt.int32
    ALU, ACT, AX = mybir.AluOpType, mybir.ActivationFunctionType, mybir.AxisListType

    P, B, F = x.shape
    C = y.shape[2]
    NB = N // P
    FULL = NB * P
    REM = N - FULL
    assert B == NB + 1
    BANKS = 8
    GW = BANKS * P
    NG = B // BANKS
    LW = N - (NG - 1) * GW
    ROUND = [4, 3, 3, 3]
    RB = sum(ROUND)
    START = [sum(ROUND[:q]) for q in range(len(ROUND))]
    Q = len(ROUND)
    ROUNDS = NB // RB
    CHUNKS = Q * ROUNDS
    WITH_ABS = (2, 4, 7, 9, 11)
    W = 2 * F + 1
    SCALE = 2048.0
    ALPHA, EPS_L1, EPS_LN = 0.1, 1e-12, 1e-5
    PART = 10
    LAB_N = 500
    RK = 500
    RC = REM * N // RK
    CHECKS = 2 * CHUNKS - len(WITH_ABS)
    BADS = NG * CHECKS + 5

    with ExitStack() as ctx:
        def sb(name, shape, dt):
            return ctx.enter_context(nc.sbuf_tensor(name, shape, dt))

        def sem(name):
            return ctx.enter_context(nc.semaphore(name))

        a_ring = sb("a_ring", [P, RB, GW], F32)
        m_ring = sb("m_ring", [P, RB, GW], BF16)
        x_sb = sb("x_sb", [P, B, F], F32)
        h0_sb = sb("h0_sb", [P, B, F], F32)
        h_full = sb("h_full", [P, 2, PART, F], F32)
        h_sb = sb("h_sb", [P, B, W], F16)
        label_row = sb("label_row", [P, N], BF16)
        scratch = sb("scratch", [P, N], F32)
        junk = [sb(f"junk{n}", [P, max(ROUND) * GW], U8) for n in range(2)]
        m_rem = sb("m_rem", [P, N], BF16)
        a_rem_check = sb("a_rem_check", [RC, RK], F32)
        y_sb = sb("y_sb", [P, B, C], F32)
        class_row = sb("class_row", [P, C], F32)
        class_col = sb("class_col", [C, 1], I32)
        class_w = sb("class_w", [C, P], BF16)
        label_col = sb("label_col", [P, B], F32)
        one_hot_sum = sb("one_hot_sum", [P, B], F32)
        stats = sb("stats", [P, B, 6], F32)
        mean = sb("mean", [P, B], F32)
        shift = sb("shift", [P, B], F32)
        var = sb("var", [P, B], F32)
        tmp = sb("tmp", [P, B], F32)
        root = sb("root", [P, B], F32)
        rstd = sb("rstd", [P, B], F32)
        bad = sb("bad", [P, BADS], F32)
        bad_seen = sb("bad_seen", [P, BADS], F32)
        bad_p = sb("bad_p", [P, 1], F32)
        ones = sb("ones", [P, P], F32)
        flag = sb("flag", [P, 1], I32)
        recip = sb("recip", [P, BANKS], F32)
        l1 = sb("l1", [P, BANKS], F32)
        ps = ctx.enter_context(nc.psum_tensor("ps", [P, BANKS, 512], F32))
        g_adj, g_m, g_abs, g_h, g_rows = (a_ring[:, s, 0:P] for s in range(5))
        g_yi, g_yj = a_ring[0:C, 5, 0:P], a_ring[0:C, 6, 0:P]
        a_rem = scratch[0:REM, :]
        ABS = max(ROUND) * GW // 2
        m_abs = scratch[:, 0:ABS].bitcast(BF16).rearrange("p (s i) -> p s i", i=GW)
        part_sb = scratch[:, ABS:ABS + BANKS * F].rearrange("p (k f) -> p k f", f=F)
        out_sb = scratch[:, ABS + BANKS * F:ABS + 2 * BANKS * F].rearrange("p (k f) -> p k f", f=F)
        y_tmp = h_full[:, 0, 0:B * C // F, :].rearrange("p b f -> p (b f)").rearrange("p (b c) -> p b c", c=C)
        yt_sb = m_ring[0:C, :, :].rearrange("c s i -> c (s i)")[:, 0:2 * N]

        y_loaded, yt_loaded, h0_loaded = sem("y_loaded"), sem("yt_loaded"), sem("h0_loaded")
        x_loaded = [sem(f"x_loaded{n}") for n in range(B // PART)]
        rem_loaded, rem_check_loaded = sem("rem_loaded"), sem("rem_check_loaded")
        a_loaded = [sem(f"a_loaded{q}") for q in range(Q)]
        classes_ready, class_w_ready = sem("classes_ready"), sem("class_w_ready")
        m_rem_cleared, ones_ready = sem("m_rem_cleared"), sem("ones_ready")
        labels_spread, label_row_ready, pool_step = sem("labels_spread"), sem("label_row_ready"), sem("pool_step")
        var_ready, root_ready, affine_ready = sem("var_ready"), sem("root_ready"), sem("affine_ready")
        relu_ready, h_ready = sem("relu_ready"), sem("h_ready")
        rem_masked, masked, abs_ready, abs_used = sem("rem_masked"), sem("masked"), sem("abs_ready"), sem("abs_used")
        checked, m_used, bank_summed, bank_read = sem("checked"), sem("m_used"), sem("bank_summed"), sem("bank_read")
        out_stored, tail_stored = sem("out_stored"), [sem(f"tail_stored{n}") for n in range(2)]
        dve_step, bad_cleared = sem("dve_step"), sem("bad_cleared")
        base_ready, l1_ready, recip_ready, hi_added = sem("base_ready"), sem("l1_ready"), sem("recip_ready"), sem("hi_added")
        bad_ready, bad_summed, flag_ready = sem("bad_ready"), sem("bad_summed"), sem("flag_ready")
        g_yi_loaded, g_loaded, g_summed = sem("g_yi_loaded"), sem("g_loaded"), sem("g_summed")
        g_yy_ready, g_m_step, g_m_ready = sem("g_yy_ready"), sem("g_m_step"), sem("g_m_ready")
        g_l1_ready, g_recip_ready, g_base_ready = sem("g_l1_ready"), sem("g_recip_ready"), sem("g_base_ready")
        g_rows_ready, g_stored = sem("g_rows_ready"), sem("g_stored")

        block = ctx.enter_context(nc.Block())

        def checks_before(c):
            return 2 * c - sum(k < c for k in WITH_ABS)

        def value(eng, v):
            return v if isinstance(v, int) else eng.snap(eng.to_reg(v))

        def wait(eng, semaphore, v):
            if not isinstance(v, int) or v > 0:
                eng.wait_ge(semaphore, v)

        def groups(eng, body):
            body(0, GW)
            with eng.Fori(1, NG - 1) as g:
                body(g, GW)
            body(NG - 1, LW)

        def ring_chunks(g):
            return [(r * Q + q, r, q, slice(START[q], START[q] + ROUND[q])) for r in range(ROUNDS) for q in range(Q)]

        def steps_of_block(eng, b, body):
            body(b * B, NB, REM)
            with eng.Fori(0, NB - 1) as t:
                body(b * B + t + 1, t, P)
            body(b * B + NB, NB - 1, P)

        def blocks(eng, body):
            with eng.Fori(0, NB) as b:
                body(b, P)
            body(NB, REM)

        def if_needed(eng, path):
            eng.wait_ge(flag_ready, 1)
            found = eng.value_load(flag[0:1, 0:1], min_val=0, max_val=1)
            with eng.If(found > 0):
                path()

        @block.sync
        def _(sp):
            sp.dma_start(yt_sb.bitcast(F32), y_t[:, :]).then_inc(yt_loaded, 16)
            sp.dma_start(y_sb[:, :, :], y[:, :, :]).then_inc(y_loaded, 16)
            for n in range(B // PART):
                bs = slice(n * PART, (n + 1) * PART)
                sp.dma_start(x_sb[:, bs, :], x[:, bs, :]).then_inc(x_loaded[n], 16)

            def load_group(g, w):
                for c, r, q, blocks in ring_chunks(g):
                    masked_before = value(sp, g * NB + (r - 1) * RB + blocks.stop)
                    checked_before = value(sp, g * CHECKS + (checks_before(c - Q + 1) if r else checks_before(c - Q + 1 + CHUNKS) - CHECKS))
                    if r or not (isinstance(g, int) and g == 0):
                        sp.wait_ge(masked, masked_before)
                        sp.wait_ge(checked, checked_before)
                    j = (r * RB + blocks.start) * P
                    sp.dma_start(a_ring[:, blocks, 0:w],
                                 adj_t[j:j + ROUND[q] * P, bass.ds(g * GW, w)].rearrange("(b p) i -> p b i", p=P),
                                 ).then_inc(a_loaded[q], 16)
                    if isinstance(g, int) and g == 0 and c == 1:
                        sp.dma_start(a_rem, adj_t[FULL:N, :]).then_inc(rem_loaded, 16)
                        sp.dma_start(a_rem_check[:, :], adj_t[FULL:N, :].rearrange("r (s k) -> (r s) k", k=RK)).then_inc(rem_check_loaded, 16)
                    if isinstance(g, int) and g == 0 and c == 2 * Q:
                        sp.dma_start(h0_sb[:, :, :], h0[:, :, :]).then_inc(h0_loaded, 16)

            groups(sp, load_group)

            half = BANKS // 2
            for n in range(2):
                sp.wait_ge(bank_read, (NG - 1) * BANKS + (n + 1) * half)
                sp.dma_start(out[:, B - BANKS + n * half:B - BANKS + (n + 1) * half, :],
                             out_sb[:, n * half:(n + 1) * half, :]).then_inc(tail_stored[n], 16)
            for n in range(2):
                sp.wait_ge(tail_stored[n], 16)

            def general_path():
                sp.wait_ge(out_stored, 16 * (NG - 1))
                sp.sem_inc(g_stored, 16)
                sp.sem_inc(g_summed, 1)

                def load_block(b, w):
                    sp.dma_start(g_yi[:, 0:w], y_t[:, bass.ds(b * P, w)]).then_inc(g_yi_loaded, 16)

                    def load_step(n, t, rows):
                        sp.wait_ge(g_summed, n + 1)
                        sp.dma_start(g_adj[0:rows, 0:w], adj_t[bass.ds(t * P, rows), bass.ds(b * P, w)]).then_inc(g_loaded, 16)
                        sp.dma_start(g_yj[:, 0:rows], y_t[:, bass.ds(t * P, rows)]).then_inc(g_loaded, 16)

                    steps_of_block(sp, b, load_step)
                    sp.wait_ge(g_rows_ready, b + 2)
                    sp.dma_start(out[:, bass.ds(b, 1), :].rearrange("p o f -> p (o f)"), g_rows).then_inc(g_stored, 16)

                blocks(sp, load_block)
                sp.wait_ge(g_stored, 16 * (B + 1))

            if_needed(sp, general_path)

        @block.gpsimd
        def _(pool):
            nc.gpsimd.iota(class_col[:, :], pattern=[[0, 1]], base=1, channel_multiplier=1).then_inc(pool_step, 1)
            pool.wait_ge(pool_step, 1)
            nc.gpsimd.tensor_copy(class_w[:, :], class_col[:, 0:1].to_broadcast([C, P])).then_inc(class_w_ready, 1)
            for c in range(C):
                last = nc.gpsimd.memset(class_row[:, c:c + 1], c + 1.0)
            last.then_inc(classes_ready, 1)
            nc.gpsimd.memset(h_sb[:, :, 2 * F:W], 1.0).then_inc(ones_ready, 1)
            nc.gpsimd.memset(ones[:, :], 1.0).then_inc(ones_ready, 1)
            nc.gpsimd.memset(m_rem[:, :], 0.0).then_inc(m_rem_cleared, 1)

            with pool.Fori(0, NG - 1) as g:
                pool.wait_ge(bank_read, (g + 1) * BANKS)
                pool.dma_start(out[:, bass.ds(g * BANKS, BANKS), :], out_sb[:, :, :]).then_inc(out_stored, 16)
            pool.wait_ge(out_stored, 16 * (NG - 1))

        @block.scalar
        def _(act):
            for k in range(N // LAB_N):
                act.wait_ge(labels_spread, k + 1)
                nc.scalar.activation(label_row[:, k * LAB_N:(k + 1) * LAB_N], ps[:, k % BANKS, 0:LAB_N],
                                     ACT.Copy).then_inc(label_row_ready, 1)

            def relu_part(n):
                wait(act, h_ready, n - 1)
                for b in range(PART):
                    c = n * PART + b
                    made = nc.scalar.activation(h_full[:, n % 2, b, :], x_sb[:, c, :], ACT.Relu,
                                                bias=shift[:, c:c + 1], scale=rstd[:, c:c + 1])
                made.then_inc(relu_ready, 1)

            def junk_writer(k):
                return k - 1 if k >= 2 else -((CHECKS - 1 - k) % 2)

            act.wait_ge(bad_cleared, 1)
            act.wait_ge(var_ready, 1)
            nc.scalar.activation(root[:, :], var[:, :], ACT.Sqrt).then_inc(root_ready, 1)
            act.wait_ge(affine_ready, 1)
            relu_part(0)

            def check_group(g, w):
                for c, r, q, blocks in ring_chunks(g):
                    act.wait_ge(a_loaded[q], 16 * (g * ROUNDS + r + 1))
                    nb = ROUND[q]
                    k = checks_before(c)
                    wait(act, checked, g * CHECKS + junk_writer(k))
                    nc.scalar.activation(junk[k % 2][:, 0:nb * w].rearrange("p (b i) -> p b i", b=nb),
                                         a_ring[:, :, :].bitcast(U16)[:, blocks, 0:2 * w:2], ACT.Copy,
                                         accum_out=bad[:, bass.ds(g * CHECKS + k, 1)]).then_inc(checked, 1)
                    if isinstance(g, int) and g == 0 and c < B // PART - 1:
                        relu_part(c + 1)
                    if c in WITH_ABS:
                        continue
                    wait(act, checked, g * CHECKS + junk_writer(k + 1))
                    nc.scalar.activation(junk[(k + 1) % 2][:, 0:nb * w].rearrange("p (b i) -> p b i", b=nb),
                                         a_ring[:, blocks, 0:w], ACT.Relu, scale=-1.0,
                                         accum_out=bad[:, bass.ds(g * CHECKS + k + 1, 1)]).then_inc(checked, 1)

            groups(act, check_group)

            rb = NG * CHECKS
            act.wait_ge(rem_check_loaded, 16)
            act.wait_ge(checked, rb)
            nc.scalar.activation(junk[0][0:RC, 0:RK], a_rem_check[:, :].bitcast(U16)[:, 0:2 * RK:2], ACT.Copy,
                                 accum_out=bad[0:RC, rb:rb + 1]).then_inc(checked, 1)
            nc.scalar.activation(junk[1][0:RC, 0:RK], a_rem_check[:, :], ACT.Relu, scale=-1.0,
                                 accum_out=bad[0:RC, rb + 1:rb + 2]).then_inc(checked, 1)

        @block.tensor
        def _(pe):
            pe.wait_ge(yt_loaded, 16)
            pe.wait_ge(class_w_ready, 1)
            for k in range(N // LAB_N):
                if k >= BANKS:
                    pe.wait_ge(label_row_ready, k - BANKS + 1)
                nc.tensor.matmul(ps[:, k % BANKS, 0:LAB_N], class_w[:, :],
                                 yt_sb[:, 2 * k * LAB_N + 1:2 * (k + 1) * LAB_N:2],
                                 start=True, stop=True).then_inc(labels_spread, 1)
            pe.wait_ge(label_row_ready, N // LAB_N)
            pe.wait_ge(ones_ready, 2)

            def sum_group(g, w):
                first = isinstance(g, int) and g == 0
                sizes = [min(P, w - P * k) for k in range(BANKS)]
                for c, r, q, blocks in ring_chunks(g):
                    width = W - 1 if c in WITH_ABS else W
                    for s in range(blocks.start, blocks.stop):
                        b = r * RB + s
                        if first and b % PART == 0:
                            pe.wait_ge(h_ready, b // PART + 1)
                        pe.wait_ge(masked, g * NB + b + 1)
                        for k, m in enumerate(sizes):
                            if b == 0:
                                wait(pe, bank_read, (g - 1) * BANKS + k + 1)
                            mm = nc.tensor.matmul(ps[0:m, k, 0:width], m_ring[:, s, k * P:k * P + m],
                                                  h_sb[:, b, 0:width], start=(b == 0), stop=False)
                        mm.then_inc(m_used, 1)
                    if c in WITH_ABS:
                        pe.wait_ge(abs_ready, g * len(WITH_ABS) + WITH_ABS.index(c) + 1)
                        for s in range(ROUND[q]):
                            for k, m in enumerate(sizes):
                                mm = nc.tensor.matmul(ps[0:m, k, W - 1:W], m_abs[:, s, k * P:k * P + m],
                                                      h_sb[:, 0, W - 1:W], start=False, stop=False)
                        mm.then_inc(abs_used, 1)
                if first:
                    pe.wait_ge(rem_masked, 1)
                for k, m in enumerate(sizes):
                    nc.tensor.matmul(ps[0:m, k, 0:W], m_rem[:, bass.ds(g * GW + k * P, m)], h_sb[:, NB, :],
                                     start=False, stop=True).then_inc(bank_summed, 1)

            groups(pe, sum_group)

            pe.wait_ge(bad_ready, 1)
            pe.wait_ge(bank_read, NG * BANKS)
            nc.tensor.matmul(ps[:, 0, 0:1], ones[:, :], bad_p[:, :], start=True, stop=True).then_inc(bad_summed, 1)

            def general_path():
                pe.sem_inc(g_rows_ready, 1)

                def sum_block(b, w):
                    pe.wait_ge(g_yi_loaded, 16 * (b + 1))

                    def sum_step(n, t, rows):
                        first, last = rows == REM, isinstance(t, int) and t == NB - 1
                        pe.wait_ge(g_loaded, 32 * (n + 1))
                        nc.tensor.matmul(ps[:, 0, 0:P], g_yj, g_yi, start=True,
                                         stop=True).then_inc(g_yy_ready, 1)
                        pe.wait_ge(g_m_ready, n + 1)
                        if first:
                            pe.wait_ge(g_rows_ready, b + 1)
                        nc.tensor.matmul(ps[:, 1, 0:F], g_m[0:rows, :], g_h[0:rows, :], start=first, stop=last)
                        nc.tensor.matmul(ps[:, 2, 0:1], g_abs[0:rows, :], ones[0:rows, 0:1], start=first,
                                         stop=last).then_inc(g_summed, 1)

                    steps_of_block(pe, b, sum_step)

                blocks(pe, sum_block)

            if_needed(pe, general_path)

        @block.vector
        def _(dve):
            steps = [0]

            def wait_own(ins):
                steps[0] += 1
                ins.then_inc(dve_step, 1)
                dve.wait_ge(dve_step, steps[0])

            nc.vector.memset(bad[:, :], 0.0).then_inc(bad_cleared, 1)
            dve.wait_ge(bad_cleared, 1)

            dve.wait_ge(y_loaded, 16)
            dve.wait_ge(classes_ready, 1)
            wait_own(nc.vector.tensor_tensor(y_tmp[:, :, :], y_sb[:, :, :],
                                             class_row[:, :].rearrange("p (o c) -> p o c", o=1).to_broadcast([P, B, C]), ALU.mult))
            wait_own(nc.vector.reduce_sum(label_col[:, :], y_tmp[:, :, :], AX.X))
            yb = NG * CHECKS + 2
            nc.vector.scalar_tensor_tensor(y_tmp[:, :, :], y_sb[:, :, :], 1.0, y_sb[:, :, :], ALU.is_equal,
                                           ALU.not_equal, accum_out=bad[:, yb:yb + 1])
            wait_own(nc.vector.reduce_sum(one_hot_sum[:, :], y_sb[:, :, :], AX.X))
            nc.vector.tensor_scalar(tmp[:, 0:NB], one_hot_sum[:, 0:NB], 1.0, 0.0, ALU.not_equal, ALU.add,
                                    accum_out=bad[:, yb + 1:yb + 2])
            wait_own(nc.vector.tensor_scalar(tmp[0:REM, NB:B], one_hot_sum[0:REM, NB:B], 1.0, 0.0, ALU.not_equal, ALU.add,
                                             accum_out=bad[0:REM, yb + 2:yb + 3]))

            for b in range(B):
                if b % PART == 0:
                    dve.wait_ge(x_loaded[b // PART], 16)
                st = nc.vector.bn_stats(stats[:, b, :], x_sb[:, b, :])
            wait_own(st)
            wait_own(nc.vector.tensor_tensor(mean[:, :], stats[:, :, 1], stats[:, :, 4], ALU.subtract))
            wait_own(nc.vector.tensor_tensor(var[:, :], mean[:, :], mean[:, :], ALU.mult))
            wait_own(nc.vector.scalar_tensor_tensor(var[:, :], var[:, :], F / 4.0, stats[:, :, 2], ALU.mult, ALU.add))
            wait_own(nc.vector.tensor_tensor(var[:, :], var[:, :], stats[:, :, 5], ALU.add))
            nc.vector.tensor_scalar(var[:, :], var[:, :], 1.0 / F, EPS_LN, ALU.mult, ALU.add).then_inc(var_ready, 1)
            wait_own(nc.vector.tensor_tensor(mean[:, :], stats[:, :, 1], stats[:, :, 4], ALU.add))
            dve.wait_ge(root_ready, 1)
            wait_own(nc.vector.reciprocal(rstd[:, :], root[:, :]))
            wait_own(nc.vector.tensor_tensor(tmp[:, :], rstd[:, :], rstd[:, :], ALU.mult))
            wait_own(nc.vector.tensor_tensor(tmp[:, :], tmp[:, :], var[:, :], ALU.mult))
            wait_own(nc.vector.tensor_scalar(tmp[:, :], tmp[:, :], -0.5 * SCALE, 1.5 * SCALE, ALU.mult, ALU.add))
            wait_own(nc.vector.tensor_tensor(rstd[:, :], rstd[:, :], tmp[:, :], ALU.mult))
            nc.vector.scalar_tensor_tensor(shift[:, :], mean[:, :], -0.5, rstd[:, :], ALU.mult,
                                           ALU.mult).then_inc(affine_ready, 1)

            def split_part(part):
                bs = slice(part * PART, (part + 1) * PART)
                full = h_full[:, part % 2, :, :]
                dve.wait_ge(relu_ready, part + 1)
                wait_own(nc.vector.tensor_copy(h_sb[:, bs, 0:F], full))
                nc.vector.tensor_tensor(h_sb[:, bs, F:2 * F], full, h_sb[:, bs, 0:F], ALU.subtract).then_inc(h_ready, 1)

            def mask_remainder():
                dve.wait_ge(m_rem_cleared, 1)
                dve.wait_ge(rem_loaded, 16)
                nc.vector.scalar_tensor_tensor(m_rem[0:REM, :], label_row[0:REM, :], label_col[0:REM, NB:B], a_rem,
                                               ALU.is_equal, ALU.mult).then_inc(rem_masked, 1)

            def finish_group(g):
                bs = bass.ds(g * BANKS, BANKS)
                dve.wait_ge(h0_loaded, 16)
                nc.vector.scalar_tensor_tensor(part_sb[:, :, :], h0_sb[:, bs, :], ALPHA, x_sb[:, bs, :], ALU.mult,
                                               ALU.add).then_inc(base_ready, 1)
                dve.wait_ge(bank_summed, (g + 1) * BANKS)
                nc.vector.tensor_scalar(l1[:, :], ps[:, :, 2 * F], EPS_L1, SCALE / (1.0 - ALPHA), ALU.max,
                                        ALU.mult).then_inc(l1_ready, 1)
                dve.wait_ge(l1_ready, g + 1)
                nc.vector.reciprocal(recip[:, :], l1[:, :]).then_inc(recip_ready, 1)
                dve.wait_ge(recip_ready, g + 1)
                dve.wait_ge(base_ready, g + 1)
                for k in range(BANKS):
                    nc.vector.scalar_tensor_tensor(part_sb[:, k, :], ps[:, k, 0:F], recip[:, k:k + 1], part_sb[:, k, :],
                                                   ALU.mult, ALU.add).then_inc(hi_added, 1)
                wait(dve, out_stored, 16 * g)
                for k in range(BANKS):
                    dve.wait_ge(hi_added, g * BANKS + k + 1)
                    nc.vector.scalar_tensor_tensor(out_sb[:, k, :], ps[:, k, F:2 * F], recip[:, k:k + 1],
                                                   part_sb[:, k, :], ALU.mult, ALU.add).then_inc(bank_read, 1)

            def mask_group(g, w):
                first = isinstance(g, int) and g == 0
                labels = label_row[:, bass.ds(g * GW, w)]
                for c, r, q, blocks in ring_chunks(g):
                    dve.wait_ge(a_loaded[q], 16 * (g * ROUNDS + r + 1))
                    for s in range(blocks.start, blocks.stop):
                        b = r * RB + s
                        wait(dve, m_used, g * NB + b - RB + 1)
                        nc.vector.scalar_tensor_tensor(m_ring[:, s, 0:w], labels, label_col[:, b:b + 1],
                                                       a_ring[:, s, 0:w], ALU.is_equal, ALU.mult).then_inc(masked, 1)
                    if c in WITH_ABS:
                        n = g * len(WITH_ABS) + WITH_ABS.index(c)
                        wait(dve, abs_used, n)
                        dve.wait_ge(masked, g * NB + r * RB + blocks.stop)
                        nc.vector.tensor_scalar(m_abs[:, 0:ROUND[q], 0:w].bitcast(U16), m_ring[:, blocks, 0:w].bitcast(U16),
                                                0x7FFF, None, ALU.bitwise_and).then_inc(abs_ready, 1)
                    if first and c < B // PART:
                        split_part(c)
                    if first and c == 1:
                        mask_remainder()
                    if not first and c == 0:
                        finish_group(g - 1)

            dve.wait_ge(label_row_ready, N // LAB_N)
            groups(dve, mask_group)
            finish_group(NG - 1)

            dve.wait_ge(checked, NG * CHECKS + 2)
            wait_own(nc.vector.tensor_scalar(bad_seen[:, :], bad[:, :], 0.0, None, ALU.not_equal))
            nc.vector.reduce_sum(bad_p[:, :], bad_seen[:, :], AX.X).then_inc(bad_ready, 1)
            dve.wait_ge(bad_summed, 1)
            nc.vector.tensor_scalar(flag[:, :], ps[:, 0, 0:1], 0.0, None, ALU.is_gt).then_inc(flag_ready, 1)

            def general_path():
                def mask_block(b, w):
                    def mask_step(n, t, rows):
                        dve.wait_ge(g_yy_ready, n + 1)
                        nc.vector.tensor_tensor(g_m[0:rows, :], g_adj[0:rows, :], ps[0:rows, 0, 0:P], ALU.mult).then_inc(g_m_step, 1)
                        nc.vector.tensor_tensor(g_h[0:rows, :], h_sb[0:rows, bass.ds(t, 1), 0:F].rearrange("p o f -> p (o f)"),
                                                h_sb[0:rows, bass.ds(t, 1), F:2 * F].rearrange("p o f -> p (o f)"), ALU.add)
                        dve.wait_ge(g_m_step, n + 1)
                        nc.vector.scalar_tensor_tensor(g_abs[0:rows, :], g_m[0:rows, :], -1.0, g_m[0:rows, :], ALU.mult, ALU.max).then_inc(g_m_ready, 1)

                    steps_of_block(dve, b, mask_step)
                    dve.wait_ge(g_summed, (b + 1) * B + 1)
                    nc.vector.tensor_scalar(l1[:, 0:1], ps[:, 2, 0:1], EPS_L1, SCALE / (1.0 - ALPHA), ALU.max,
                                            ALU.mult).then_inc(g_l1_ready, 1)
                    dve.wait_ge(g_l1_ready, b + 1)
                    nc.vector.reciprocal(recip[:, 0:1], l1[:, 0:1]).then_inc(g_recip_ready, 1)
                    nc.vector.scalar_tensor_tensor(part_sb[:, 0, :], h0_sb[:, bass.ds(b, 1), :].rearrange("p o f -> p (o f)"),
                                                   ALPHA, x_sb[:, bass.ds(b, 1), :].rearrange("p o f -> p (o f)"),
                                                   ALU.mult, ALU.add).then_inc(g_base_ready, 1)
                    dve.wait_ge(g_base_ready, b + 1)
                    dve.wait_ge(g_recip_ready, b + 1)
                    dve.wait_ge(g_stored, 16 * (b + 1))
                    nc.vector.scalar_tensor_tensor(g_rows[:, :], ps[:, 1, 0:F], recip[:, 0:1],
                                                   part_sb[:, 0, :], ALU.mult, ALU.add).then_inc(g_rows_ready, 1)

                blocks(dve, mask_block)

            if_needed(dve, general_path)


def kernel(x, adj, L0_gnn_h0, L0_gnn_y):
    import numpy as np
    import concourse.bacc as bacc
    from concourse import mybir
    from concourse.bass_utils import run_bass_kernel_spmd

    x, adj, h0, y = (np.asarray(a) for a in (x, adj, L0_gnn_h0, L0_gnn_y))
    n, p = x.shape[0], 128
    blocks = -(-n // p)

    def in_blocks(a):
        full = np.zeros((blocks * p, a.shape[1]), a.dtype)
        full[:n] = a
        return np.ascontiguousarray(full.reshape(blocks, p, -1).transpose(1, 0, 2))

    nc = bacc.Bacc("TRN2", target_bir_lowering=False, num_devices=1)
    arrays = {
        "x": in_blocks(x),
        "adj_t": np.ascontiguousarray(adj.T),
        "h0": in_blocks(h0),
        "y": in_blocks(y),
        "y_t": np.ascontiguousarray(y.T),
    }
    handles = [nc.dram_tensor(name, a.shape, mybir.dt.from_np(a.dtype), kind="ExternalInput").ap()
               for name, a in arrays.items()]
    handles.append(nc.dram_tensor("result", arrays["x"].shape, mybir.dt.float32, kind="ExternalOutput").ap())
    build_masked_adjacency(nc, *handles, N=n)
    got = run_bass_kernel_spmd(nc, [arrays], core_ids=[0])
    return got.results[0]["result"].transpose(1, 0, 2).reshape(blocks * p, -1)[:n]
```

```python
from contextlib import ExitStack

import concourse.bass as bass
from concourse import mybir


def build_masked_adjacency(nc, x, adj_t, h0, y, y_t, out, *, N):
    F32, BF16, F16 = mybir.dt.float32, mybir.dt.bfloat16, mybir.dt.float16
    U8, U16, I32 = mybir.dt.uint8, mybir.dt.uint16, mybir.dt.int32
    ALU, ACT, AX = mybir.AluOpType, mybir.ActivationFunctionType, mybir.AxisListType

    P, B, F = x.shape
    C = y.shape[2]
    NB = N // P
    FULL = NB * P
    REM = N - FULL
    assert B == NB + 1
    BANKS = 8
    HALF = BANKS // 2
    GW = BANKS * P
    NG = B // BANKS
    LW = N - (NG - 1) * GW
    ROUND = [3, 4, 3, 3]
    RB = sum(ROUND)
    START = [sum(ROUND[:q]) for q in range(len(ROUND))]
    Q = len(ROUND)
    ROUNDS = NB // RB
    CHUNKS = Q * ROUNDS
    WITH_ABS = (1, 3, 5, 7, 9)
    W = 2 * F + 1
    SCALE = 2048.0
    ALPHA, EPS_L1, EPS_LN = 0.1, 1e-12, 1e-5
    PART = 10
    RELU_AT, SPLIT_AT = (0, 1, 3, 5), (1, 2, 4, 6)
    LAB_N = 500
    RK = 500
    RC = REM * N // RK
    CHECKS = 2 * CHUNKS - len(WITH_ABS)
    BADS = NG * CHECKS + 5

    with ExitStack() as ctx:
        def sb(name, shape, dt):
            return ctx.enter_context(nc.sbuf_tensor(name, shape, dt))

        def sem(name):
            return ctx.enter_context(nc.semaphore(name))

        a_ring = sb("a_ring", [P, RB, GW], F32)
        m_ring = sb("m_ring", [P, RB, GW], BF16)
        x_sb = sb("x_sb", [P, B, F], F32)
        h0_sb = sb("h0_sb", [P, B, F], F32)
        h_full = sb("h_full", [P, 2, PART, F], F32)
        h_sb = sb("h_sb", [P, B, W], F16)
        label_row = sb("label_row", [P, N], BF16)
        m_abs = sb("m_abs", [P, max(ROUND), GW], BF16)
        part_sb = sb("part_sb", [P, BANKS, F], F32)
        out_sb = sb("out_sb", [P, BANKS, F], F32)
        junk = [sb(f"junk{n}", [P, max(ROUND) * GW], U8) for n in range(2)]
        m_rem = sb("m_rem", [P, N], BF16)
        rem_adj = sb("rem_adj", [RC, RK], F32)
        rem_label_col = sb("rem_label_col", [RC, 1], F32)
        rem_labels = sb("rem_labels", [RC, RK], BF16)
        rem_m = sb("rem_m", [RC, RK], BF16)
        y_sb = sb("y_sb", [P, B, C], F32)
        class_row = sb("class_row", [P, C], F32)
        class_col = sb("class_col", [C, 1], I32)
        class_w = sb("class_w", [C, P], BF16)
        label_col = sb("label_col", [P, B], F32)
        one_hot_sum = sb("one_hot_sum", [P, B], F32)
        stats = sb("stats", [P, B, 6], F32)
        mean = sb("mean", [P, B], F32)
        shift = sb("shift", [P, B], F32)
        var = sb("var", [P, B], F32)
        tmp = sb("tmp", [P, B], F32)
        root = sb("root", [P, B], F32)
        rstd = sb("rstd", [P, B], F32)
        bad = sb("bad", [P, BADS], F32)
        bad_seen = sb("bad_seen", [P, BADS], F32)
        bad_p = sb("bad_p", [P, 1], F32)
        ones = sb("ones", [P, P], F32)
        flag = sb("flag", [P, 1], I32)
        recip = sb("recip", [P, BANKS], F32)
        l1 = sb("l1", [P, BANKS], F32)
        ps = ctx.enter_context(nc.psum_tensor("ps", [P, BANKS, 512], F32))
        g_adj, g_m, g_abs, g_h, g_rows = (a_ring[:, s, 0:P] for s in range(5))
        g_yi, g_yj = a_ring[0:C, 5, 0:P], a_ring[0:C, 6, 0:P]
        y_tmp = h_full[:, 0, 0:B * C // F, :].rearrange("p b f -> p (b f)").rearrange("p (b c) -> p b c", c=C)
        yt_sb = m_ring[0:C, :, :].rearrange("c s i -> c (s i)")[:, 0:2 * N]

        y_loaded, yt_loaded, h0_loaded = sem("y_loaded"), sem("yt_loaded"), sem("h0_loaded")
        x_loaded = [sem(f"x_loaded{n}") for n in range(B // PART)]
        rem_loaded, rem_placed = sem("rem_loaded"), sem("rem_placed")
        rem_labels_placed, rem_label_placed = sem("rem_labels_placed"), sem("rem_label_placed")
        a_loaded = [sem(f"a_loaded{q}") for q in range(Q)]
        classes_ready, class_w_ready = sem("classes_ready"), sem("class_w_ready")
        label_col_ready = sem("label_col_ready")
        m_rem_cleared, ones_ready = sem("m_rem_cleared"), sem("ones_ready")
        labels_spread, label_row_ready, pool_step = sem("labels_spread"), sem("label_row_ready"), sem("pool_step")
        var_ready, root_ready, affine_ready = sem("var_ready"), sem("root_ready"), sem("affine_ready")
        relu_ready, h_ready = sem("relu_ready"), sem("h_ready")
        rem_masked, masked, abs_ready, abs_used = sem("rem_masked"), sem("masked"), sem("abs_ready"), sem("abs_used")
        checked, m_used, rows_ready = sem("checked"), sem("m_used"), sem("rows_ready")
        out_stored, tail_stored = sem("out_stored"), [sem(f"tail_stored{n}") for n in range(2)]
        dve_step, bad_cleared = sem("dve_step"), sem("bad_cleared")
        base_ready, l1_ready, recip_ready = sem("base_ready"), sem("l1_ready"), sem("recip_ready")
        hi_added = sem("hi_added")
        bad_ready, bad_summed, flag_ready = sem("bad_ready"), sem("bad_summed"), sem("flag_ready")
        g_yi_loaded, g_loaded, g_summed = sem("g_yi_loaded"), sem("g_loaded"), sem("g_summed")
        g_yy_ready, g_m_step, g_m_ready = sem("g_yy_ready"), sem("g_m_step"), sem("g_m_ready")
        g_l1_ready, g_recip_ready, g_base_ready = sem("g_l1_ready"), sem("g_recip_ready"), sem("g_base_ready")
        g_rows_ready, g_stored = sem("g_rows_ready"), sem("g_stored")

        block = ctx.enter_context(nc.Block())

        def checks_before(c):
            return 2 * c - sum(k < c for k in WITH_ABS)

        def value(eng, v):
            return v if isinstance(v, int) else eng.snap(eng.to_reg(v))

        def wait(eng, semaphore, v):
            if not isinstance(v, int) or v > 0:
                eng.wait_ge(semaphore, v)

        def groups(eng, body):
            body(0, GW)
            with eng.Fori(1, NG - 1) as g:
                body(g, GW)
            body(NG - 1, LW)

        def ring_chunks(g):
            return [(r * Q + q, r, q, slice(START[q], START[q] + ROUND[q])) for r in range(ROUNDS) for q in range(Q)]

        def steps_of_block(eng, b, body):
            body(b * B, NB, REM)
            with eng.Fori(0, NB - 1) as t:
                body(b * B + t + 1, t, P)
            body(b * B + NB, NB - 1, P)

        def blocks(eng, body):
            with eng.Fori(0, NB) as b:
                body(b, P)
            body(NB, REM)

        def if_needed(eng, path):
            eng.wait_ge(flag_ready, 1)
            found = eng.value_load(flag[0:1, 0:1], min_val=0, max_val=1)
            with eng.If(found > 0):
                path()

        @block.sync
        def _(sp):
            sp.dma_start(y_sb[:, :, :], y[:, :, :]).then_inc(y_loaded, 16)
            sp.dma_start(yt_sb.bitcast(F32), y_t[:, :]).then_inc(yt_loaded, 16)
            for n in range(B // PART):
                bs = slice(n * PART, (n + 1) * PART)
                sp.dma_start(x_sb[:, bs, :], x[:, bs, :]).then_inc(x_loaded[n], 16)
            def load_group(g, w):
                for c, r, q, blocks in ring_chunks(g):
                    masked_before = value(sp, g * NB + (r - 1) * RB + blocks.stop)
                    through = checks_before(c - Q + 1) if r else checks_before(c - Q + 1 + CHUNKS) - CHECKS
                    checked_before = value(sp, g * CHECKS + through)
                    if r or not (isinstance(g, int) and g == 0):
                        sp.wait_ge(masked, masked_before)
                        sp.wait_ge(checked, checked_before)
                    j = (r * RB + blocks.start) * P
                    sp.dma_start(a_ring[:, blocks, 0:w],
                                 adj_t[j:j + ROUND[q] * P, bass.ds(g * GW, w)].rearrange("(b p) i -> p b i", p=P),
                                 ).then_inc(a_loaded[q], 16)
                    if isinstance(g, int) and g == 0 and c == 0:
                        sp.dma_start(rem_adj[:, :], adj_t[FULL:N, :].rearrange("r (s k) -> (r s) k", k=RK),
                                     ).then_inc(rem_loaded, 16)
                    if isinstance(g, int) and g == 0 and c == 2 * Q:
                        sp.dma_start(h0_sb[:, :, :], h0[:, :, :]).then_inc(h0_loaded, 16)

            groups(sp, load_group)

            for n in range(2):
                sp.wait_ge(rows_ready, (NG - 1) * BANKS + (n + 1) * HALF)
                sp.dma_start(out[:, B - BANKS + n * HALF:B - BANKS + (n + 1) * HALF, :],
                             out_sb[:, n * HALF:(n + 1) * HALF, :]).then_inc(tail_stored[n], 16)
            for n in range(2):
                sp.wait_ge(tail_stored[n], 16)

            def general_path():
                sp.wait_ge(out_stored, 16 * (NG - 1))
                sp.sem_inc(g_stored, 16)
                sp.sem_inc(g_summed, 1)

                def load_block(b, w):
                    sp.dma_start(g_yi[:, 0:w], y_t[:, bass.ds(b * P, w)]).then_inc(g_yi_loaded, 16)

                    def load_step(n, t, rows):
                        sp.wait_ge(g_summed, n + 1)
                        sp.dma_start(g_adj[0:rows, 0:w], adj_t[bass.ds(t * P, rows), bass.ds(b * P, w)],
                                     ).then_inc(g_loaded, 16)
                        sp.dma_start(g_yj[:, 0:rows], y_t[:, bass.ds(t * P, rows)]).then_inc(g_loaded, 16)

                    steps_of_block(sp, b, load_step)
                    sp.wait_ge(g_rows_ready, b + 2)
                    sp.dma_start(out[:, bass.ds(b, 1), :].rearrange("p o f -> p (o f)"), g_rows).then_inc(g_stored, 16)

                blocks(sp, load_block)
                sp.wait_ge(g_stored, 16 * (B + 1))

            if_needed(sp, general_path)

        @block.gpsimd
        def _(pool):
            nc.gpsimd.iota(class_col[:, :], pattern=[[0, 1]], base=1, channel_multiplier=1).then_inc(pool_step, 1)
            pool.wait_ge(pool_step, 1)
            nc.gpsimd.tensor_copy(class_w[:, :], class_col[:, 0:1].to_broadcast([C, P])).then_inc(class_w_ready, 1)
            for c in range(C):
                last = nc.gpsimd.memset(class_row[:, c:c + 1], c + 1.0)
            last.then_inc(classes_ready, 1)
            nc.gpsimd.memset(h_sb[:, :, 2 * F:W], 1.0).then_inc(ones_ready, 1)
            nc.gpsimd.memset(ones[:, :], 1.0).then_inc(ones_ready, 1)
            nc.gpsimd.memset(m_rem[:, :], 0.0).then_inc(m_rem_cleared, 1)

            pool.wait_ge(m_rem_cleared, 1)
            pool.wait_ge(rem_masked, 1)
            pool.dma_start(m_rem[0:REM, :].rearrange("r (s k) -> r s k", k=RK), rem_m[:, :]).then_inc(rem_placed, 16)

            with pool.Fori(0, NG - 1) as g:
                pool.wait_ge(rows_ready, (g + 1) * BANKS)
                pool.dma_start(out[:, bass.ds(g * BANKS, BANKS), :], out_sb[:, :, :]).then_inc(out_stored, 16)
            pool.wait_ge(out_stored, 16 * (NG - 1))

        @block.scalar
        def _(act):
            for k in range(N // LAB_N):
                act.wait_ge(labels_spread, k + 1)
                nc.scalar.activation(label_row[:, k * LAB_N:(k + 1) * LAB_N], ps[:, k % BANKS, 0:LAB_N],
                                     ACT.Copy).then_inc(label_row_ready, 1)

            act.wait_ge(label_row_ready, N // LAB_N)
            act.dma_start(rem_labels[:, :], label_row[0:REM, :].rearrange("r (s k) -> r s k", k=RK),
                          ).then_inc(rem_labels_placed, 16)
            act.wait_ge(label_col_ready, 1)
            act.dma_start(rem_label_col[:, :],
                          label_col[0:REM, NB:B].rearrange("r (s k) -> r s k", s=1).to_broadcast([REM, RC // REM, 1]),
                          ).then_inc(rem_label_placed, 16)

            def relu_part(n):
                act.wait_ge(affine_ready, 1)
                wait(act, h_ready, n - 1)
                for b in range(PART):
                    c = n * PART + b
                    made = nc.scalar.activation(h_full[:, n % 2, b, :], x_sb[:, c, :], ACT.Relu,
                                                bias=shift[:, c:c + 1], scale=rstd[:, c:c + 1])
                made.then_inc(relu_ready, 1)

            def junk_writer(k):
                return k - 1 if k >= 2 else -((CHECKS - 1 - k) % 2)

            act.wait_ge(bad_cleared, 1)
            act.wait_ge(var_ready, 1)
            nc.scalar.activation(root[:, :], var[:, :], ACT.Sqrt).then_inc(root_ready, 1)

            def check_signs(g, w, k, blocks):
                wait(act, checked, g * CHECKS + junk_writer(k))
                nc.scalar.activation(junk[k % 2][:, 0:(blocks.stop - blocks.start) * w].rearrange("p (b i) -> p b i", i=w),
                                     a_ring[:, blocks, 0:w], ACT.Relu, scale=-1.0,
                                     accum_out=bad[:, bass.ds(g * CHECKS + k, 1)]).then_inc(checked, 1)

            def check_group(g, w):
                for c, r, q, blocks in ring_chunks(g):
                    act.wait_ge(a_loaded[q], 16 * (g * ROUNDS + r + 1))
                    nb = ROUND[q]
                    k = checks_before(c)
                    wait(act, checked, g * CHECKS + junk_writer(k))
                    nc.scalar.activation(junk[k % 2][:, 0:nb * w].rearrange("p (b i) -> p b i", b=nb),
                                         a_ring[:, :, :].bitcast(U16)[:, blocks, 0:2 * w:2], ACT.Copy,
                                         accum_out=bad[:, bass.ds(g * CHECKS + k, 1)]).then_inc(checked, 1)
                    if isinstance(g, int) and g == 0 and c in RELU_AT:
                        relu_part(RELU_AT.index(c))
                    if c not in WITH_ABS:
                        check_signs(g, w, k + 1, blocks)

            groups(act, check_group)

            rb = NG * CHECKS
            act.wait_ge(rem_loaded, 16)
            act.wait_ge(checked, rb)
            nc.scalar.activation(junk[0][0:RC, 0:RK], rem_adj[:, :].bitcast(U16)[:, 0:2 * RK:2], ACT.Copy,
                                 accum_out=bad[0:RC, rb:rb + 1]).then_inc(checked, 1)
            nc.scalar.activation(junk[1][0:RC, 0:RK], rem_adj[:, :], ACT.Relu, scale=-1.0,
                                 accum_out=bad[0:RC, rb + 1:rb + 2]).then_inc(checked, 1)

        @block.tensor
        def _(pe):
            pe.wait_ge(yt_loaded, 16)
            pe.wait_ge(class_w_ready, 1)
            for k in range(N // LAB_N):
                if k >= BANKS:
                    pe.wait_ge(label_row_ready, k - BANKS + 1)
                nc.tensor.matmul(ps[:, k % BANKS, 0:LAB_N], class_w[:, :],
                                 yt_sb[:, 2 * k * LAB_N + 1:2 * (k + 1) * LAB_N:2],
                                 start=True, stop=True).then_inc(labels_spread, 1)
            pe.wait_ge(label_row_ready, N // LAB_N)
            pe.wait_ge(ones_ready, 2)

            def sum_group(g, w):
                first = isinstance(g, int) and g == 0
                sizes = [min(P, w - P * k) for k in range(BANKS)]
                for c, r, q, blocks in ring_chunks(g):
                    width = W - 1 if c in WITH_ABS else W
                    for s in range(blocks.start, blocks.stop):
                        b = r * RB + s
                        if first and b % PART == 0:
                            pe.wait_ge(h_ready, b // PART + 1)
                        if b == 0:
                            wait(pe, rows_ready, BANKS * g)
                        pe.wait_ge(masked, g * NB + b + 1)
                        for k, m in enumerate(sizes):
                            mm = nc.tensor.matmul(ps[0:m, k, 0:width], m_ring[:, s, k * P:k * P + m],
                                                  h_sb[:, b, 0:width], start=(b == 0), stop=(b == NB - 1))
                        mm.then_inc(m_used, 1)
                    if c in WITH_ABS:
                        pe.wait_ge(abs_ready, g * len(WITH_ABS) + WITH_ABS.index(c) + 1)
                        for s in range(ROUND[q]):
                            for k, m in enumerate(sizes):
                                mm = nc.tensor.matmul(ps[0:m, k, W - 1:W], m_abs[:, s, k * P:k * P + m],
                                                      h_sb[:, 0, W - 1:W], start=False, stop=False)
                        mm.then_inc(abs_used, 1)
                    if c == CHUNKS - 2:
                        if first:
                            pe.wait_ge(rem_placed, 16)
                        for k, m in enumerate(sizes):
                            nc.tensor.matmul(ps[0:m, k, 0:W], m_rem[:, bass.ds(g * GW + k * P, m)], h_sb[:, NB, :],
                                             start=False, stop=False)

            groups(pe, sum_group)

            pe.wait_ge(bad_ready, 1)
            pe.wait_ge(rows_ready, BANKS * NG)
            nc.tensor.matmul(ps[:, 0, 0:1], ones[:, :], bad_p[:, :], start=True, stop=True).then_inc(bad_summed, 1)

            def general_path():
                pe.sem_inc(g_rows_ready, 1)

                def sum_block(b, w):
                    pe.wait_ge(g_yi_loaded, 16 * (b + 1))

                    def sum_step(n, t, rows):
                        first, last = rows == REM, isinstance(t, int) and t == NB - 1
                        pe.wait_ge(g_loaded, 32 * (n + 1))
                        nc.tensor.matmul(ps[:, 0, 0:P], g_yj, g_yi, start=True,
                                         stop=True).then_inc(g_yy_ready, 1)
                        pe.wait_ge(g_m_ready, n + 1)
                        if first:
                            pe.wait_ge(g_rows_ready, b + 1)
                        nc.tensor.matmul(ps[:, 1, 0:F], g_m[0:rows, :], g_h[0:rows, :], start=first, stop=last)
                        nc.tensor.matmul(ps[:, 2, 0:1], g_abs[0:rows, :], ones[0:rows, 0:1], start=first,
                                         stop=last).then_inc(g_summed, 1)

                    steps_of_block(pe, b, sum_step)

                blocks(pe, sum_block)

            if_needed(pe, general_path)

        @block.vector
        def _(dve):
            steps = [0]

            def wait_own(ins):
                steps[0] += 1
                ins.then_inc(dve_step, 1)
                dve.wait_ge(dve_step, steps[0])

            nc.vector.memset(bad[:, :], 0.0).then_inc(bad_cleared, 1)
            dve.wait_ge(bad_cleared, 1)

            dve.wait_ge(y_loaded, 16)
            dve.wait_ge(classes_ready, 1)
            classes = class_row[:, :].rearrange("p (o c) -> p o c", o=1).to_broadcast([P, B, C])
            wait_own(nc.vector.tensor_tensor(y_tmp[:, :, :], y_sb[:, :, :], classes, ALU.mult))
            nc.vector.reduce_sum(label_col[:, :], y_tmp[:, :, :], AX.X).then_inc(label_col_ready, 1)
            dve.wait_ge(label_col_ready, 1)
            yb = NG * CHECKS + 2
            nc.vector.scalar_tensor_tensor(y_tmp[:, :, :], y_sb[:, :, :], 1.0, y_sb[:, :, :], ALU.is_equal,
                                           ALU.not_equal, accum_out=bad[:, yb:yb + 1])
            wait_own(nc.vector.reduce_sum(one_hot_sum[:, :], y_sb[:, :, :], AX.X))
            nc.vector.tensor_scalar(tmp[:, 0:NB], one_hot_sum[:, 0:NB], 1.0, 0.0, ALU.not_equal, ALU.add,
                                    accum_out=bad[:, yb + 1:yb + 2])
            wait_own(nc.vector.tensor_scalar(tmp[0:REM, NB:B], one_hot_sum[0:REM, NB:B], 1.0, 0.0, ALU.not_equal, ALU.add,
                                             accum_out=bad[0:REM, yb + 2:yb + 3]))

            def find_variance():
                for b in range(B):
                    if b % PART == 0:
                        dve.wait_ge(x_loaded[b // PART], 16)
                    st = nc.vector.bn_stats(stats[:, b, :], x_sb[:, b, :])
                wait_own(st)
                wait_own(nc.vector.tensor_tensor(mean[:, :], stats[:, :, 1], stats[:, :, 4], ALU.subtract))
                wait_own(nc.vector.tensor_tensor(var[:, :], mean[:, :], mean[:, :], ALU.mult))
                wait_own(nc.vector.scalar_tensor_tensor(var[:, :], var[:, :], F / 4.0, stats[:, :, 2], ALU.mult, ALU.add))
                wait_own(nc.vector.tensor_tensor(var[:, :], var[:, :], stats[:, :, 5], ALU.add))
                nc.vector.tensor_scalar(var[:, :], var[:, :], 1.0 / F, EPS_LN, ALU.mult, ALU.add).then_inc(var_ready, 1)
                wait_own(nc.vector.tensor_tensor(mean[:, :], stats[:, :, 1], stats[:, :, 4], ALU.add))

            def find_affine():
                dve.wait_ge(root_ready, 1)
                wait_own(nc.vector.reciprocal(rstd[:, :], root[:, :]))
                wait_own(nc.vector.tensor_tensor(tmp[:, :], rstd[:, :], rstd[:, :], ALU.mult))
                wait_own(nc.vector.tensor_tensor(tmp[:, :], tmp[:, :], var[:, :], ALU.mult))
                wait_own(nc.vector.tensor_scalar(tmp[:, :], tmp[:, :], -0.5 * SCALE, 1.5 * SCALE, ALU.mult, ALU.add))
                wait_own(nc.vector.tensor_tensor(rstd[:, :], rstd[:, :], tmp[:, :], ALU.mult))
                nc.vector.scalar_tensor_tensor(shift[:, :], mean[:, :], -0.5, rstd[:, :], ALU.mult,
                                               ALU.mult).then_inc(affine_ready, 1)

            def split_part(part):
                bs = slice(part * PART, (part + 1) * PART)
                full = h_full[:, part % 2, :, :]
                dve.wait_ge(relu_ready, part + 1)
                wait_own(nc.vector.tensor_copy(h_sb[:, bs, 0:F], full))
                nc.vector.tensor_tensor(h_sb[:, bs, F:2 * F], full, h_sb[:, bs, 0:F], ALU.subtract).then_inc(h_ready, 1)

            def mask_remainder():
                dve.wait_ge(rem_loaded, 16)
                dve.wait_ge(rem_labels_placed, 16)
                dve.wait_ge(rem_label_placed, 16)
                nc.vector.scalar_tensor_tensor(rem_m[:, :], rem_labels[:, :], rem_label_col[:, 0:1], rem_adj[:, :],
                                               ALU.is_equal, ALU.mult).then_inc(rem_masked, 1)

            def finish_group(g):
                bs = bass.ds(g * BANKS, BANKS)
                dve.wait_ge(h0_loaded, 16)
                wait(dve, rows_ready, BANKS * g)
                nc.vector.scalar_tensor_tensor(part_sb[:, :, :], h0_sb[:, bs, :], ALPHA, x_sb[:, bs, :], ALU.mult,
                                               ALU.add).then_inc(base_ready, 1)
                dve.wait_ge(m_used, (g + 1) * NB)
                nc.vector.tensor_scalar(l1[:, :], ps[:, :, 2 * F], EPS_L1, SCALE / (1.0 - ALPHA), ALU.max,
                                        ALU.mult).then_inc(l1_ready, 1)
                dve.wait_ge(l1_ready, g + 1)
                nc.vector.reciprocal(recip[:, :], l1[:, :]).then_inc(recip_ready, 1)
                wait(dve, out_stored, 16 * g)
                dve.wait_ge(recip_ready, g + 1)
                dve.wait_ge(base_ready, g + 1)
                for k in range(BANKS):
                    nc.vector.scalar_tensor_tensor(part_sb[:, k, :], ps[:, k, 0:F], recip[:, k:k + 1], part_sb[:, k, :],
                                                   ALU.mult, ALU.add).then_inc(hi_added, 1)
                for k in range(BANKS):
                    dve.wait_ge(hi_added, g * BANKS + k + 1)
                    nc.vector.scalar_tensor_tensor(out_sb[:, k, :], ps[:, k, F:2 * F], recip[:, k:k + 1],
                                                   part_sb[:, k, :], ALU.mult, ALU.add).then_inc(rows_ready, 1)

            def make_abs(g, w, c, place):
                r, blocks = place
                n = g * len(WITH_ABS) + WITH_ABS.index(c)
                wait(dve, abs_used, n)
                dve.wait_ge(masked, g * NB + r * RB + blocks.stop)
                nc.vector.tensor_scalar(m_abs[:, 0:blocks.stop - blocks.start, 0:w].bitcast(U16),
                                        m_ring[:, blocks, 0:w].bitcast(U16), 0x7FFF, None,
                                        ALU.bitwise_and).then_inc(abs_ready, 1)

            def mask_group(g, w):
                first = isinstance(g, int) and g == 0
                labels = label_row[:, bass.ds(g * GW, w)]
                previous = None
                for c, r, q, blocks in ring_chunks(g):
                    dve.wait_ge(a_loaded[q], 16 * (g * ROUNDS + r + 1))
                    if (c - Q) % CHUNKS in WITH_ABS:
                        held = WITH_ABS.index((c - Q) % CHUNKS) + 1 - (0 if r else len(WITH_ABS))
                        wait(dve, abs_ready, g * len(WITH_ABS) + held)
                    for s in range(blocks.start, blocks.stop):
                        b = r * RB + s
                        wait(dve, m_used, g * NB + b - RB + 1)
                        nc.vector.scalar_tensor_tensor(m_ring[:, s, 0:w], labels, label_col[:, b:b + 1],
                                                       a_ring[:, s, 0:w], ALU.is_equal, ALU.mult).then_inc(masked, 1)
                        if s == blocks.start and c - 1 in WITH_ABS:
                            make_abs(g, w, c - 1, previous)
                    previous = r, blocks
                    if first and c == 0:
                        find_affine()
                    if first and c == 2:
                        mask_remainder()
                    if first and c in SPLIT_AT:
                        split_part(SPLIT_AT.index(c))
                    if not first and c == 0:
                        finish_group(g - 1)

            find_variance()
            dve.wait_ge(label_row_ready, N // LAB_N)
            groups(dve, mask_group)
            finish_group(NG - 1)

            dve.wait_ge(checked, NG * CHECKS + 2)
            wait_own(nc.vector.tensor_scalar(bad_seen[:, :], bad[:, :], 0.0, None, ALU.not_equal))
            nc.vector.reduce_sum(bad_p[:, :], bad_seen[:, :], AX.X).then_inc(bad_ready, 1)
            dve.wait_ge(bad_summed, 1)
            nc.vector.tensor_scalar(flag[:, :], ps[:, 0, 0:1], 0.0, None, ALU.is_gt).then_inc(flag_ready, 1)

            def general_path():
                def mask_block(b, w):
                    def mask_step(n, t, rows):
                        dve.wait_ge(g_yy_ready, n + 1)
                        nc.vector.tensor_tensor(g_m[0:rows, :], g_adj[0:rows, :], ps[0:rows, 0, 0:P],
                                                ALU.mult).then_inc(g_m_step, 1)
                        nc.vector.tensor_tensor(g_h[0:rows, :], h_sb[0:rows, bass.ds(t, 1), 0:F].rearrange("p o f -> p (o f)"),
                                                h_sb[0:rows, bass.ds(t, 1), F:2 * F].rearrange("p o f -> p (o f)"), ALU.add)
                        dve.wait_ge(g_m_step, n + 1)
                        nc.vector.scalar_tensor_tensor(g_abs[0:rows, :], g_m[0:rows, :], -1.0, g_m[0:rows, :],
                                                       ALU.mult, ALU.max).then_inc(g_m_ready, 1)

                    steps_of_block(dve, b, mask_step)
                    dve.wait_ge(g_summed, (b + 1) * B + 1)
                    nc.vector.tensor_scalar(l1[:, 0:1], ps[:, 2, 0:1], EPS_L1, SCALE / (1.0 - ALPHA), ALU.max,
                                            ALU.mult).then_inc(g_l1_ready, 1)
                    dve.wait_ge(g_l1_ready, b + 1)
                    nc.vector.reciprocal(recip[:, 0:1], l1[:, 0:1]).then_inc(g_recip_ready, 1)
                    nc.vector.scalar_tensor_tensor(part_sb[:, 0, :], h0_sb[:, bass.ds(b, 1), :].rearrange("p o f -> p (o f)"),
                                                   ALPHA, x_sb[:, bass.ds(b, 1), :].rearrange("p o f -> p (o f)"),
                                                   ALU.mult, ALU.add).then_inc(g_base_ready, 1)
                    dve.wait_ge(g_base_ready, b + 1)
                    dve.wait_ge(g_recip_ready, b + 1)
                    dve.wait_ge(g_stored, 16 * (b + 1))
                    nc.vector.scalar_tensor_tensor(g_rows[:, :], ps[:, 1, 0:F], recip[:, 0:1],
                                                   part_sb[:, 0, :], ALU.mult, ALU.add).then_inc(g_rows_ready, 1)

                blocks(dve, mask_block)

            if_needed(dve, general_path)


def kernel(x, adj, L0_gnn_h0, L0_gnn_y):
    import numpy as np
    import concourse.bacc as bacc
    from concourse import mybir
    from concourse.bass_utils import run_bass_kernel_spmd

    x, adj, h0, y = (np.asarray(a) for a in (x, adj, L0_gnn_h0, L0_gnn_y))
    n, p = x.shape[0], 128
    blocks = -(-n // p)

    def in_blocks(a):
        full = np.zeros((blocks * p, a.shape[1]), a.dtype)
        full[:n] = a
        return np.ascontiguousarray(full.reshape(blocks, p, -1).transpose(1, 0, 2))

    nc = bacc.Bacc("TRN2", target_bir_lowering=False, num_devices=1)
    arrays = {
        "x": in_blocks(x),
        "adj_t": np.ascontiguousarray(adj.T),
        "h0": in_blocks(h0),
        "y": in_blocks(y),
        "y_t": np.ascontiguousarray(y.T),
    }
    handles = [nc.dram_tensor(name, a.shape, mybir.dt.from_np(a.dtype), kind="ExternalInput").ap()
               for name, a in arrays.items()]
    handles.append(nc.dram_tensor("result", arrays["x"].shape, mybir.dt.float32, kind="ExternalOutput").ap())
    build_masked_adjacency(nc, *handles, N=n)
    got = run_bass_kernel_spmd(nc, [arrays], core_ids=[0])
    return got.results[0]["result"].transpose(1, 0, 2).reshape(blocks * p, -1)[:n]
```
